# Optimizing a Trainium2 kernel written in Bass

```python
import numpy as np
import jax
import jax.numpy as jnp

def _softmax(x, axis=-1):
    return jax.nn.softmax(x, axis=axis)

def _gelu(x):
    return jax.nn.gelu(x, approximate=True)

def _silu(x):
    return jax.nn.silu(x)

def _sigmoid(x):
    return jax.nn.sigmoid(x)

def _layernorm(x, axis=-1, eps=1e-05):
    m = jnp.mean(x, axis=axis, keepdims=True)
    v = jnp.var(x, axis=axis, keepdims=True)
    return (x - m) / jnp.sqrt(v + eps)

def _scatter_add(tgt, idx, src, axis=0):
    return tgt.at[idx].add(src)

def _segment_sum(src, seg, n):
    return jax.ops.segment_sum(src, seg, n)
kernel_name = 'mk_dlrm_tower_d1_rec_r8_48d76f'

def setup_inputs(seed: int=0):
    np.random.seed(seed)
    _w = jnp.asarray

    def _rec_inputs():
        import jax
        import jax.numpy as jnp
        _tk = jax.random.key(seed)
        dense_ctx = jax.random.normal(jax.random.fold_in(_tk, 190), (1024, 16), jnp.float32)
        ids = jnp.stack([jax.random.randint(jax.random.fold_in(_tk, 200 + f), (1024,), 0, v, jnp.int32) for f, v in enumerate([1250, 1250, 1250, 1000, 125000, 125000, 1250, 125000, 1250, 12500, 12500, 1250, 12500, 1000, 12500, 12500, 12500, 1000, 12500, 1000, 1250, 1000, 1250, 1250, 1250, 1250, 1250, 1000, 1250, 1250, 1000, 1250, 1250, 1250, 1000, 1250, 1250, 1000, 1000, 1000])], axis=1)
        tbl_0 = 0.05 * jax.random.normal(jax.random.fold_in(_tk, 500 + 0), (1250, 64), jnp.float32)
        tbl_1 = 0.05 * jax.random.normal(jax.random.fold_in(_tk, 500 + 1), (1250, 64), jnp.float32)
        tbl_2 = 0.05 * jax.random.normal(jax.random.fold_in(_tk, 500 + 2), (1250, 64), jnp.float32)
        tbl_3 = 0.05 * jax.random.normal(jax.random.fold_in(_tk, 500 + 3), (1000, 64), jnp.float32)
        tbl_4 = 0.05 * jax.random.normal(jax.random.fold_in(_tk, 500 + 4), (125000, 64), jnp.float32)
        tbl_5 = 0.05 * jax.random.normal(jax.random.fold_in(_tk, 500 + 5), (125000, 64), jnp.float32)
        tbl_6 = 0.05 * jax.random.normal(jax.random.fold_in(_tk, 500 + 6), (1250, 64), jnp.float32)
        tbl_7 = 0.05 * jax.random.normal(jax.random.fold_in(_tk, 500 + 7), (125000, 64), jnp.float32)
        tbl_8 = 0.05 * jax.random.normal(jax.random.fold_in(_tk, 500 + 8), (1250, 64), jnp.float32)
        tbl_9 = 0.05 * jax.random.normal(jax.random.fold_in(_tk, 500 + 9), (12500, 64), jnp.float32)
        tbl_10 = 0.05 * jax.random.normal(jax.random.fold_in(_tk, 500 + 10), (12500, 64), jnp.float32)
        tbl_11 = 0.05 * jax.random.normal(jax.random.fold_in(_tk, 500 + 11), (1250, 64), jnp.float32)
        tbl_12 = 0.05 * jax.random.normal(jax.random.fold_in(_tk, 500 + 12), (12500, 64), jnp.float32)
        tbl_13 = 0.05 * jax.random.normal(jax.random.fold_in(_tk, 500 + 13), (1000, 64), jnp.float32)
        tbl_14 = 0.05 * jax.random.normal(jax.random.fold_in(_tk, 500 + 14), (12500, 64), jnp.float32)
        tbl_15 = 0.05 * jax.random.normal(jax.random.fold_in(_tk, 500 + 15), (12500, 64), jnp.float32)
        tbl_16 = 0.05 * jax.random.normal(jax.random.fold_in(_tk, 500 + 16), (12500, 64), jnp.float32)
        tbl_17 = 0.05 * jax.random.normal(jax.random.fold_in(_tk, 500 + 17), (1000, 64), jnp.float32)
        tbl_18 = 0.05 * jax.random.normal(jax.random.fold_in(_tk, 500 + 18), (12500, 64), jnp.float32)
        tbl_19 = 0.05 * jax.random.normal(jax.random.fold_in(_tk, 500 + 19), (1000, 64), jnp.float32)
        tbl_20 = 0.05 * jax.random.normal(jax.random.fold_in(_tk, 500 + 20), (1250, 64), jnp.float32)
        tbl_21 = 0.05 * jax.random.normal(jax.random.fold_in(_tk, 500 + 21), (1000, 64), jnp.float32)
        tbl_22 = 0.05 * jax.random.normal(jax.random.fold_in(_tk, 500 + 22), (1250, 64), jnp.float32)
        tbl_23 = 0.05 * jax.random.normal(jax.random.fold_in(_tk, 500 + 23), (1250, 64), jnp.float32)
        tbl_24 = 0.05 * jax.random.normal(jax.random.fold_in(_tk, 500 + 24), (1250, 64), jnp.float32)
        tbl_25 = 0.05 * jax.random.normal(jax.random.fold_in(_tk, 500 + 25), (1250, 64), jnp.float32)
        tbl_26 = 0.05 * jax.random.normal(jax.random.fold_in(_tk, 500 + 26), (1250, 64), jnp.float32)
        tbl_27 = 0.05 * jax.random.normal(jax.random.fold_in(_tk, 500 + 27), (1000, 64), jnp.float32)
        tbl_28 = 0.05 * jax.random.normal(jax.random.fold_in(_tk, 500 + 28), (1250, 64), jnp.float32)
        tbl_29 = 0.05 * jax.random.normal(jax.random.fold_in(_tk, 500 + 29), (1250, 64), jnp.float32)
        tbl_30 = 0.05 * jax.random.normal(jax.random.fold_in(_tk, 500 + 30), (1000, 64), jnp.float32)
        tbl_31 = 0.05 * jax.random.normal(jax.random.fold_in(_tk, 500 + 31), (1250, 64), jnp.float32)
        tbl_32 = 0.05 * jax.random.normal(jax.random.fold_in(_tk, 500 + 32), (1250, 64), jnp.float32)
        tbl_33 = 0.05 * jax.random.normal(jax.random.fold_in(_tk, 500 + 33), (1250, 64), jnp.float32)
        tbl_34 = 0.05 * jax.random.normal(jax.random.fold_in(_tk, 500 + 34), (1000, 64), jnp.float32)
        tbl_35 = 0.05 * jax.random.normal(jax.random.fold_in(_tk, 500 + 35), (1250, 64), jnp.float32)
        tbl_36 = 0.05 * jax.random.normal(jax.random.fold_in(_tk, 500 + 36), (1250, 64), jnp.float32)
        tbl_37 = 0.05 * jax.random.normal(jax.random.fold_in(_tk, 500 + 37), (1000, 64), jnp.float32)
        tbl_38 = 0.05 * jax.random.normal(jax.random.fold_in(_tk, 500 + 38), (1000, 64), jnp.float32)
        tbl_39 = 0.05 * jax.random.normal(jax.random.fold_in(_tk, 500 + 39), (1000, 64), jnp.float32)
        _rk = jax.random.fold_in(_tk, 7)
        W_top1 = 0.0354441 * jax.random.normal(jax.random.fold_in(_tk, 801), (796, 512), jnp.float32)
        W_top2 = 0.0441942 * jax.random.normal(jax.random.fold_in(_tk, 802), (512, 256), jnp.float32)
        W_top3 = 0.0625 * jax.random.normal(jax.random.fold_in(_tk, 803), (256, 1), jnp.float32)
        b_top1 = jnp.zeros((512,), jnp.float32)
        b_top2 = jnp.zeros((256,), jnp.float32)
        return (dense_ctx, ids, tbl_0, tbl_1, tbl_2, tbl_3, tbl_4, tbl_5, tbl_6, tbl_7, tbl_8, tbl_9, tbl_10, tbl_11, tbl_12, tbl_13, tbl_14, tbl_15, tbl_16, tbl_17, tbl_18, tbl_19, tbl_20, tbl_21, tbl_22, tbl_23, tbl_24, tbl_25, tbl_26, tbl_27, tbl_28, tbl_29, tbl_30, tbl_31, tbl_32, tbl_33, tbl_34, tbl_35, tbl_36, tbl_37, tbl_38, tbl_39, W_top1, b_top1, W_top2, b_top2, W_top3)
    dense_ctx, ids, tbl_0, tbl_1, tbl_2, tbl_3, tbl_4, tbl_5, tbl_6, tbl_7, tbl_8, tbl_9, tbl_10, tbl_11, tbl_12, tbl_13, tbl_14, tbl_15, tbl_16, tbl_17, tbl_18, tbl_19, tbl_20, tbl_21, tbl_22, tbl_23, tbl_24, tbl_25, tbl_26, tbl_27, tbl_28, tbl_29, tbl_30, tbl_31, tbl_32, tbl_33, tbl_34, tbl_35, tbl_36, tbl_37, tbl_38, tbl_39, W_top1, b_top1, W_top2, b_top2, W_top3 = _rec_inputs()

    def _L0_rec_setup():
        import jax, jax.numpy as jnp
        import numpy as np
        NUM_FIELDS = 40
        EMBED = 64
        BATCH = 512
        NUM_PAIRS = NUM_FIELDS * (NUM_FIELDS - 1) // 2
        _ROW, _COL = np.triu_indices(NUM_FIELDS, k=1)
        key = jax.random.key(seed)
        k1, k2 = jax.random.split(key)
        feat_emb = jax.random.normal(k1, (BATCH, NUM_FIELDS, EMBED), dtype=jnp.float32)
        kernel = jax.random.normal(k2, (EMBED, NUM_PAIRS, EMBED), dtype=jnp.float32) * 0.05
        return {'feat_emb': feat_emb, 'kernel': kernel}
    _L0_rec_all = _L0_rec_setup()
    _L0_rec_in = {k: v for k, v in _L0_rec_all.items() if k in ('kernel',)}
    del _L0_rec_all
    return {'dense_ctx': dense_ctx, 'ids': ids, 'tbl_0': tbl_0, 'tbl_1': tbl_1, 'tbl_2': tbl_2, 'tbl_3': tbl_3, 'tbl_4': tbl_4, 'tbl_5': tbl_5, 'tbl_6': tbl_6, 'tbl_7': tbl_7, 'tbl_8': tbl_8, 'tbl_9': tbl_9, 'tbl_10': tbl_10, 'tbl_11': tbl_11, 'tbl_12': tbl_12, 'tbl_13': tbl_13, 'tbl_14': tbl_14, 'tbl_15': tbl_15, 'tbl_16': tbl_16, 'tbl_17': tbl_17, 'tbl_18': tbl_18, 'tbl_19': tbl_19, 'tbl_20': tbl_20, 'tbl_21': tbl_21, 'tbl_22': tbl_22, 'tbl_23': tbl_23, 'tbl_24': tbl_24, 'tbl_25': tbl_25, 'tbl_26': tbl_26, 'tbl_27': tbl_27, 'tbl_28': tbl_28, 'tbl_29': tbl_29, 'tbl_30': tbl_30, 'tbl_31': tbl_31, 'tbl_32': tbl_32, 'tbl_33': tbl_33, 'tbl_34': tbl_34, 'tbl_35': tbl_35, 'tbl_36': tbl_36, 'tbl_37': tbl_37, 'tbl_38': tbl_38, 'tbl_39': tbl_39, 'W_top1': W_top1, 'b_top1': b_top1, 'W_top2': W_top2, 'b_top2': b_top2, 'W_top3': W_top3, 'L0_rec_kernel': _L0_rec_in['kernel']}

def reference(dense_ctx, ids, tbl_0, tbl_1, tbl_2, tbl_3, tbl_4, tbl_5, tbl_6, tbl_7, tbl_8, tbl_9, tbl_10, tbl_11, tbl_12, tbl_13, tbl_14, tbl_15, tbl_16, tbl_17, tbl_18, tbl_19, tbl_20, tbl_21, tbl_22, tbl_23, tbl_24, tbl_25, tbl_26, tbl_27, tbl_28, tbl_29, tbl_30, tbl_31, tbl_32, tbl_33, tbl_34, tbl_35, tbl_36, tbl_37, tbl_38, tbl_39, W_top1, b_top1, W_top2, b_top2, W_top3, L0_rec_kernel):
    import jax
    import jax.numpy as jnp

    def _L0_rec_ref(feat_emb, kernel):
        import jax, jax.numpy as jnp
        import numpy as np
        NUM_FIELDS = 40
        EMBED = 64
        BATCH = 512
        NUM_PAIRS = NUM_FIELDS * (NUM_FIELDS - 1) // 2
        _ROW, _COL = np.triu_indices(NUM_FIELDS, k=1)
        row = jnp.asarray(_ROW)
        col = jnp.asarray(_COL)
        p = feat_emb[:, row]
        q = feat_emb[:, col]
        out = jnp.einsum('bpk,epk,bpe->bp', p, kernel, q)
        return out
    e = jnp.stack([tbl_0[ids[:, 0]], tbl_1[ids[:, 1]], tbl_2[ids[:, 2]], tbl_3[ids[:, 3]], tbl_4[ids[:, 4]], tbl_5[ids[:, 5]], tbl_6[ids[:, 6]], tbl_7[ids[:, 7]], tbl_8[ids[:, 8]], tbl_9[ids[:, 9]], tbl_10[ids[:, 10]], tbl_11[ids[:, 11]], tbl_12[ids[:, 12]], tbl_13[ids[:, 13]], tbl_14[ids[:, 14]], tbl_15[ids[:, 15]], tbl_16[ids[:, 16]], tbl_17[ids[:, 17]], tbl_18[ids[:, 18]], tbl_19[ids[:, 19]], tbl_20[ids[:, 20]], tbl_21[ids[:, 21]], tbl_22[ids[:, 22]], tbl_23[ids[:, 23]], tbl_24[ids[:, 24]], tbl_25[ids[:, 25]], tbl_26[ids[:, 26]], tbl_27[ids[:, 27]], tbl_28[ids[:, 28]], tbl_29[ids[:, 29]], tbl_30[ids[:, 30]], tbl_31[ids[:, 31]], tbl_32[ids[:, 32]], tbl_33[ids[:, 33]], tbl_34[ids[:, 34]], tbl_35[ids[:, 35]], tbl_36[ids[:, 36]], tbl_37[ids[:, 37]], tbl_38[ids[:, 38]], tbl_39[ids[:, 39]]], axis=1)
    z = _L0_rec_ref(e, L0_rec_kernel)
    z = z.reshape(z.shape[0], -1)
    h = jnp.concatenate([z, dense_ctx], axis=1)
    h = jnp.maximum(h @ W_top1 + b_top1, 0.0)
    h = jnp.maximum(h @ W_top2 + b_top2, 0.0)
    y = h @ W_top3
    return y

_drawn_inputs = setup_inputs


def setup_inputs(seed=0):
    import zlib

    import numpy as np

    out = dict(_drawn_inputs(seed))
    spreads = {'b_top1': (0.0, 0.1), 'b_top2': (0.0, 0.1)}
    factors = {'tbl_0': 6.374,
     'tbl_1': 6.103,
     'tbl_2': 6.071,
     'tbl_3': 5.341,
     'tbl_4': 6.011,
     'tbl_5': 5.272,
     'tbl_6': 6.035,
     'tbl_7': 5.794,
     'tbl_8': 5.528,
     'tbl_9': 5.132,
     'tbl_10': 5.653,
     'tbl_11': 6.293,
     'tbl_12': 5.391,
     'tbl_13': 5.494,
     'tbl_14': 5.668,
     'tbl_15': 5.902,
     'tbl_16': 5.934,
     'tbl_17': 5.394,
     'tbl_18': 6.342,
     'tbl_19': 5.876,
     'tbl_20': 5.571,
     'tbl_21': 6.268,
     'tbl_22': 5.739,
     'tbl_23': 5.57,
     'tbl_24': 6.136,
     'tbl_25': 5.864,
     'tbl_26': 5.29,
     'tbl_27': 6.263,
     'tbl_28': 5.691,
     'tbl_29': 5.811,
     'tbl_30': 5.746,
     'tbl_31': 5.36,
     'tbl_32': 6.094,
     'tbl_33': 5.486,
     'tbl_34': 5.611,
     'tbl_35': 5.692,
     'tbl_36': 6.151,
     'tbl_37': 6.391,
     'tbl_38': 6.124,
     'tbl_39': 5.719}
    for name, (base, spread) in spreads.items():
        noise = np.random.default_rng([zlib.crc32(name.encode()), seed]).standard_normal(out[name].shape)
        drawn = base * np.exp(spread * noise) if base else spread * noise
        out[name] = jnp.asarray(drawn.astype(out[name].dtype))
    for name, factor in factors.items():
        out[name] = (out[name] * factor).astype(out[name].dtype)
    return out
```

```python
from contextlib import ExitStack

import numpy as np

import concourse.bass as bass
from concourse import mybir

P = 128
FIELDS, EMBED, BATCH = 40, 64, 1024
DENSE, HID1, HID2 = 16, 512, 256
BLOCKS = FIELDS // 2
HALF = 512
HALVES = BATCH // HALF
BTILES = BATCH // P
QUAD = 4
GROUP = 16 * QUAD
CHUNK = 4
STEP_COLS = 2 * P

RAW_RING, X_RING, Y_RING = 4, 2, 8
R_RING, HL_RING = 3, 2


def pair_index(i, j):
    return i * (2 * FIELDS - i - 1) // 2 + (j - i - 1)


def plan():
    steps, tiles = [], []
    for n in range(BLOCKS):
        if n % 2:
            steps.append(("diag", n, n, len(tiles)))
            tiles.append([(2 * n - 2, 2 * n - 1), (2 * n, 2 * n + 1)])
        for m in range(n):
            steps.append(("full", n, m, len(tiles)))
            tiles.append([(2 * m, 2 * n), (2 * m + 1, 2 * n)])
            tiles.append([(2 * m, 2 * n + 1), (2 * m + 1, 2 * n + 1)])
    return steps, tiles


STEPS, TILES = plan()
NSTEPS, NTILES = len(STEPS), len(TILES)
CHUNKS = NSTEPS // CHUNK
QUADS = -(-NTILES // QUAD)
GROUPS = -(-NTILES // GROUP)
DENSE_ROW = P - DENSE
SEL = 32 - 2
assert NSTEPS % CHUNK == 0


def z_row(q):
    return q // GROUP, 32 * (q % QUAD) + 2 * ((q % GROUP) // QUAD)


def turn_steps():
    first = [next((s for s, x in enumerate(STEPS) if x[1] == n), 0) for n in range(BLOCKS)]
    out = [0, 0]
    for n in range(2, BLOCKS):
        ahead = 0 if n <= 6 else 2
        out.append(first[n] - ahead)
    return out


TURN = turn_steps()


def build(nc, dense_t, ids, tables, w1, b1, w2, b2, w3, kstream, consts, out):
    F32, F32R, I32 = mybir.dt.float32, mybir.dt.float32r, mybir.dt.int32
    ALU, ACT = mybir.AluOpType, mybir.ActivationFunctionType

    with ExitStack() as ctx:
        def sb(name, shape, dt=F32):
            return ctx.enter_context(nc.sbuf_tensor(name, shape, dt))

        def sem(name):
            return ctx.enter_context(nc.semaphore(name))

        cst = sb("cst", [P, P + SEL + 32])
        ident = cst[:, 0:P]
        sel = cst[:, P:P + SEL + 32]
        idx = sb("idx", [P, BTILES, FIELDS], I32)
        raw = sb("raw", [P, RAW_RING, BTILES, P])
        emb = sb("emb", [P, BLOCKS, BATCH])
        diag_emb = sb("diag_emb", [P, BATCH])
        x = sb("x", [P, X_RING, 2, BATCH], F32R)
        k_raw = sb("k_raw", [P, R_RING, CHUNK, STEP_COLS])
        k_hi = sb("k_hi", [P, HL_RING, CHUNK, STEP_COLS], F32R)
        k_lo = sb("k_lo", [P, HL_RING, CHUNK, STEP_COLS], F32R)
        y = sb("y", [P, Y_RING, BATCH])
        z = sb("z", [P, GROUPS, BATCH])
        w3_sb = sb("w3_sb", [P, HID2 // P])
        b1_sb = sb("b1_sb", [P, HID1 // P])
        b2_sb = sb("b2_sb", [P, HID2 // P])
        out_sb = y[0:1, 0, :]
        w1_sb = raw[:, :, :, :].rearrange("p r t c -> p (r t c)")[:, 0:GROUPS * HID1].rearrange(
            "p (g n) -> p g n", g=GROUPS)
        w2_sb = emb[:, BLOCKS - 1, :].rearrange("p (k n) -> p k n", n=HID2)
        h1 = emb[:, 0:HID1 // P, :]
        h2 = emb[:, HID1 // P:HID1 // P + HID2 // P, :]

        prod = [ctx.enter_context(nc.psum_tensor(f"prod{i}", [P, BATCH], F32)) for i in range(2)]
        zsum = ctx.enter_context(nc.psum_tensor("zsum", [P, BATCH], F32))
        turned = ctx.enter_context(nc.psum_tensor("turned", [P, BATCH], F32))

        idx_in = sem("idx_in")
        const_in = sem("const_in")
        small_in = sem("small_in")
        w1_in = sem("w1_in")
        w2_in = sem("w2_in")
        gathered = [sem(f"gathered{i}") for i in range(RAW_RING)]
        k_in = [sem(f"k_in{i}") for i in range(R_RING)]
        khi_ready = sem("khi_ready")
        klo_ready = sem("klo_ready")
        block_turned = sem("block_turned")
        emb_ready = sem("emb_ready")
        block_saved = sem("block_saved")
        xhi_ready = sem("xhi_ready")
        xlo_ready = sem("xlo_ready")
        prod_ready = sem("prod_ready")
        y_ready = sem("y_ready")
        quad_summed = sem("quad_summed")
        z_saved = sem("z_saved")
        h_acc = sem("h_acc")
        h_ready = sem("h_ready")
        out_done = sem("out_done")

        def steps_tiles(s):
            return STEPS[s][3] if s < NSTEPS else NTILES

        def tiles_before_block(n):
            return next((STEPS[s][3] for s in range(NSTEPS) if STEPS[s][1] >= n), NTILES)

        block = ctx.enter_context(nc.Block())

        @block.sync
        def _(sp):
            sp.dma_start(idx[:, :, :], ids.rearrange("(t p) f -> p t f", p=P)).then_inc(idx_in, 16)
            sp.dma_start(cst[:, :], consts).then_inc(const_in, 16)
            for c in range(CHUNKS):
                if c >= R_RING:
                    sp.wait_ge(klo_ready, c - R_RING + 1)
                for h in range(2):
                    sp.dma_start(k_raw[64 * h:64 * h + 64, c % R_RING, :, :],
                                 kstream[:, c, :, :]).then_inc(k_in[c % R_RING], 16)
                if c == 2:
                    sp.dma_start(z[DENSE_ROW:P, GROUPS - 1, :], dense_t).then_inc(small_in, 16)
                    sp.dma_start(w3_sb[:, :], w3).then_inc(small_in, 16)
                    sp.dma_start(b1_sb[:, :], b1).then_inc(small_in, 16)
                    sp.dma_start(b2_sb[:, :], b2).then_inc(small_in, 16)
            sp.wait_ge(block_turned, BLOCKS)
            sp.dma_start(w1_sb, w1).then_inc(w1_in, 16)
            sp.wait_ge(xlo_ready, 2 * BLOCKS)
            sp.dma_start(w2_sb, w2).then_inc(w2_in, 16)
            sp.wait_ge(h_ready, 2 * (HID1 // P + HID2 // P) + HALVES)
            sp.dma_start(out, out_sb).then_inc(out_done, 16)
            sp.wait_ge(out_done, 16)

        @block.gpsimd
        def _(pool):
            pool.wait_ge(idx_in, 16)
            for n in range(BLOCKS):
                if n >= RAW_RING:
                    pool.wait_ge(block_turned, n - RAW_RING + 1)
                for t in range(BTILES):
                    for f in range(2):
                        pool.indirect_dma_start(
                            raw[:, n % RAW_RING, t, EMBED * f:EMBED * (f + 1)], None, tables[2 * n + f],
                            bass.IndirectOffsetOnAxis(ap=idx[:, t, 2 * n + f:2 * n + f + 1], axis=0),
                        ).then_inc(gathered[n % RAW_RING], 16)

        @block.tensor
        def _(pe):
            pe.wait_ge(const_in, 16)

            def turn(n):
                pe.wait_ge(gathered[n % RAW_RING], 16 * 2 * BTILES * (n // RAW_RING + 1))
                if n:
                    pe.wait_ge(block_saved, n)
                for t in range(BTILES):
                    last = pe.transpose(turned[:, P * t:P * (t + 1)], raw[:, n % RAW_RING, t, :], ident)
                last.then_inc(block_turned, 1)

            def product(q, passes):
                if q >= 2:
                    pe.wait_ge(y_ready, q - 1)
                acc = prod[q % 2]
                for i, (w, mov) in enumerate(passes):
                    for h in range(HALVES):
                        last = pe.matmul(acc[:, HALF * h:HALF * (h + 1)], w, mov[:, HALF * h:HALF * (h + 1)],
                                         start=(i == 0), stop=(i == len(passes) - 1))
                last.then_inc(prod_ready, 1)

            def reduce_quad(k):
                tiles = range(QUAD * k, min(QUAD * (k + 1), NTILES))
                g, slot = QUAD * k // GROUP, (QUAD * k % GROUP) // QUAD
                if slot == 0 and g:
                    pe.wait_ge(z_saved, g)
                pe.wait_ge(y_ready, tiles[-1] + 1)
                for h in range(HALVES):
                    for q in tiles:
                        c = 32 * (q % QUAD)
                        last = pe.matmul(zsum[c:c + 32, HALF * h:HALF * (h + 1)],
                                         sel[:, SEL - 2 * slot:SEL - 2 * slot + 32],
                                         y[:, q % Y_RING, HALF * h:HALF * (h + 1)],
                                         start=(slot == 0), stop=(q + QUAD >= min(NTILES, GROUP * (g + 1))),
                                         tile_position=(0, c))
                last.then_inc(quad_summed, 1)

            turn(0)
            turn(1)
            quads = 0
            for s, (kind, n, m, q) in enumerate(STEPS):
                for nn in range(2, BLOCKS):
                    if TURN[nn] == s:
                        turn(nn)
                c = s // CHUNK
                if s % CHUNK == 0:
                    pe.wait_ge(klo_ready, c + 1)
                if s == 0 or STEPS[s - 1][1] != n:
                    pe.wait_ge(xlo_ready, 2 * n + 2)
                hi, lo = (k[:, c % HL_RING, s % CHUNK, :] for k in (k_hi, k_lo))
                if kind == "full":
                    for f in range(2):
                        cols = slice(P * f, P * (f + 1))
                        mov = x[:, n % X_RING, f, :]
                        product(q + f, [(hi[:, cols], mov), (lo[:, cols], mov)])
                else:
                    passes = []
                    for f in range(2):
                        cols = slice(P * f, P * (f + 1))
                        mov = x[:, (n - 1 + f) % X_RING, 1, :]
                        passes += [(hi[:, cols], mov), (lo[:, cols], mov)]
                    product(q, passes)
                done = steps_tiles(s + 1)
                while QUAD * (quads + 1) <= done - 2:
                    reduce_quad(quads)
                    quads += 1
            while quads < QUADS:
                reduce_quad(quads)
                quads += 1

            pe.wait_ge(small_in, 16 * 4)
            pe.wait_ge(w1_in, 16)
            pe.wait_ge(w2_in, 16)
            banks = [prod[0][:, 0:HALF], prod[0][:, HALF:], prod[1][:, 0:HALF], prod[1][:, HALF:]]
            accs = 0

            def layer(w, src, rows, h, k_tiles, out_rows, need):
                nonlocal accs
                pe.wait_ge(*need)
                if accs >= 4:
                    pe.wait_ge(h_ready, accs - 3)
                for k in range(k_tiles):
                    last = pe.matmul(banks[accs % 4][0:out_rows, :], w[:, k, rows],
                                     src[:, k, HALF * h:HALF * (h + 1)], start=(k == 0), stop=(k == k_tiles - 1))
                last.then_inc(h_acc, 1)
                accs += 1

            for h in range(HALVES):
                for m in range(HID1 // P):
                    layer(w1_sb, z, slice(P * m, P * (m + 1)), h, GROUPS, P, (z_saved, GROUPS))
            for h in range(HALVES):
                for m in range(HID2 // P):
                    layer(w2_sb, h1, slice(P * m, P * (m + 1)), h, HID1 // P, P, (h_ready, HID1 // P * (h + 1)))
            w3_v = w3_sb[:, :].rearrange("p (k o) -> p k o", o=1)
            for h in range(HALVES):
                layer(w3_v, h2, slice(0, 1), h, HID2 // P, 1, (h_ready, 2 * HID1 // P + HID2 // P * (h + 1)))

        @block.scalar
        def _(act):
            def split_k(c):
                act.wait_ge(k_in[c % R_RING], 32 * (c // R_RING + 1))
                if c >= HL_RING:
                    act.wait_ge(prod_ready, steps_tiles(CHUNK * (c - HL_RING + 1)))
                act.copy(k_hi[:, c % HL_RING, :, :], k_raw[:, c % R_RING, :, :]).then_inc(khi_ready, 1)

            def save_block(n):
                act.wait_ge(block_turned, n + 1)
                if n >= X_RING:
                    act.wait_ge(prod_ready, tiles_before_block(n - 1) + (n % 2 == 0))
                act.copy(emb[:, n, :], turned[:, :]).then_inc(emb_ready, 1)
                for f in range(2):
                    rows = slice(64 * f, 64 * f + 64)
                    act.copy(x[rows, n % X_RING, f, :], turned[rows, :]).then_inc(xhi_ready, 1)
                r = slice(64 * (n % 2), 64 * (n % 2) + 64)
                if n >= 2 and n % 2 == 0:
                    act.wait_ge(y_ready, tiles_before_block(n - 1) + 1)
                act.copy(diag_emb[r, :], turned[0:64, :]).then_inc(block_saved, 1)

            def save_z(g):
                act.wait_ge(quad_summed, min(GROUP // QUAD * (g + 1), QUADS))
                rows = P if g < GROUPS - 1 else DENSE_ROW
                act.copy(z[0:rows, g, :], zsum[0:rows, :]).then_inc(z_saved, 1)

            split_k(0)
            split_k(1)
            save_block(0)
            save_block(1)
            groups = 0
            for s in range(NSTEPS):
                if s % CHUNK == 2 and s // CHUNK + 1 >= 2 and s // CHUNK + 1 < CHUNKS:
                    split_k(s // CHUNK + 1)
                for nn in range(2, BLOCKS):
                    if TURN[nn] == s:
                        save_block(nn)
                while groups < GROUPS - 1 and GROUP * (groups + 1) <= steps_tiles(s + 1) - 4:
                    save_z(groups)
                    groups += 1
            while groups < GROUPS:
                save_z(groups)
                groups += 1

            banks = [prod[0][:, 0:HALF], prod[0][:, HALF:], prod[1][:, 0:HALF], prod[1][:, HALF:]]
            accs = 0
            for dst, bias, mtiles in ((h1, b1_sb, HID1 // P), (h2, b2_sb, HID2 // P)):
                for h in range(HALVES):
                    for m in range(mtiles):
                        act.wait_ge(h_acc, accs + 1)
                        act.activation(dst[:, m, HALF * h:HALF * (h + 1)], banks[accs % 4], ACT.Relu,
                                       bias=bias[:, m:m + 1]).then_inc(h_ready, 1)
                        accs += 1
            for h in range(HALVES):
                act.wait_ge(h_acc, accs + 1)
                act.copy(out_sb[:, HALF * h:HALF * (h + 1)], banks[accs % 4][0:1, :]).then_inc(h_ready, 1)
                accs += 1

        @block.vector
        def _(dve):
            def split_k(c):
                dve.wait_ge(khi_ready, c + 1)
                dve.tensor_tensor(k_lo[:, c % HL_RING, :, :], k_raw[:, c % R_RING, :, :],
                                  k_hi[:, c % HL_RING, :, :].bitcast(F32), ALU.subtract).then_inc(klo_ready, 1)

            def save_block(n):
                for f in range(2):
                    a, b = slice(64 * f, 64 * f + 64), slice(64 - 64 * f, 128 - 64 * f)
                    dve.wait_ge(emb_ready, n + 1)
                    dve.wait_ge(xhi_ready, 2 * n + f + 1)
                    dve.tensor_tensor(x[b, n % X_RING, f, :], emb[a, n, :], x[a, n % X_RING, f, :].bitcast(F32),
                                      ALU.subtract).then_inc(xlo_ready, 1)

            def multiply(q, e):
                dve.wait_ge(prod_ready, q + 1)
                if q >= Y_RING:
                    dve.wait_ge(quad_summed, (q - Y_RING) // QUAD + 1)
                dve.tensor_tensor(y[:, q % Y_RING, :], prod[q % 2][:, :], e, ALU.mult).then_inc(y_ready, 1)

            split_k(0)
            split_k(1)
            save_block(0)
            save_block(1)
            for s, (kind, n, m, q) in enumerate(STEPS):
                if s % CHUNK == 2 and s // CHUNK + 1 >= 2 and s // CHUNK + 1 < CHUNKS:
                    split_k(s // CHUNK + 1)
                for nn in range(2, BLOCKS):
                    if TURN[nn] == s:
                        save_block(nn)
                if kind == "full":
                    dve.wait_ge(emb_ready, m + 1)
                    for f in range(2):
                        multiply(q + f, emb[:, m, :])
                else:
                    dve.wait_ge(block_saved, n + 1)
                    multiply(q, diag_emb[:, :])


def kernel(**inputs):
    import concourse.bacc as bacc
    from concourse.bass_utils import run_bass_kernel_spmd

    a = {k: np.asarray(v) for k, v in inputs.items()}
    K = a["L0_rec_kernel"]
    kstream = np.zeros((EMBED, NSTEPS, 2, 2, EMBED), K.dtype)
    for s, (kind, n, m, q) in enumerate(STEPS):
        if kind == "full":
            for f in range(2):
                for r in range(2):
                    kstream[:, s, f, r] = K[:, pair_index(*TILES[q + f][r])]
        else:
            for f in range(2):
                kstream[:, s, f, f] = K[:, pair_index(*TILES[q][f])]
    kstream = kstream.reshape(EMBED, CHUNKS, CHUNK, STEP_COLS)
    W1 = a["W_top1"]
    w1 = np.zeros((P, GROUPS, HID1), W1.dtype)
    for q, pairs in enumerate(TILES):
        g, row = z_row(q)
        for r in range(2):
            w1[row + r, g] = W1[pair_index(*pairs[r])]
    w1[DENSE_ROW:, GROUPS - 1] = W1[-DENSE:]
    consts = np.zeros((P, P + SEL + 32), np.float32)
    consts[:, 0:P] = np.eye(P, dtype=np.float32)
    for r in range(2):
        consts[64 * r:64 * r + 64, P + SEL + r] = 1.0

    def chunks(w, n):
        return np.ascontiguousarray(w.reshape(n, P, -1).transpose(1, 0, 2))

    arrays = {
        "dense_t": np.ascontiguousarray(a["dense_ctx"].T),
        "ids": a["ids"],
        "w1": w1,
        "b1": np.ascontiguousarray(a["b_top1"].reshape(-1, P).T),
        "w2": chunks(a["W_top2"], HID1 // P),
        "b2": np.ascontiguousarray(a["b_top2"].reshape(-1, P).T),
        "w3": np.ascontiguousarray(a["W_top3"].reshape(-1, P).T),
        "kstream": kstream,
        "consts": consts,
    }
    for f in range(FIELDS):
        arrays[f"tbl_{f}"] = a[f"tbl_{f}"]
    nc = bacc.Bacc("TRN2", target_bir_lowering=False, num_devices=1)
    h = {k: nc.dram_tensor(k, v.shape, mybir.dt.from_np(v.dtype), kind="ExternalInput").ap()
         for k, v in arrays.items()}
    out = nc.dram_tensor("out", (BATCH, 1), mybir.dt.float32, kind="ExternalOutput").ap()
    build(nc, h["dense_t"], h["ids"], [h[f"tbl_{f}"] for f in range(FIELDS)], h["w1"], h["b1"], h["w2"],
          h["b2"], h["w3"], h["kstream"], h["consts"], out.rearrange("b o -> o b"))
    got = run_bass_kernel_spmd(nc, [arrays], core_ids=[0])
    return got.results[0]["out"]
```

```python
from contextlib import ExitStack

import numpy as np

import concourse.bass as bass
from concourse import mybir

P = 128
FIELDS, EMBED, BATCH = 40, 64, 1024
DENSE, HID1, HID2 = 16, 512, 256
BLOCKS = FIELDS // 2
HALF = 512
HALVES = BATCH // HALF
BTILES = BATCH // P
QUAD = 4
GROUP = 16 * QUAD
CHUNK = 4
STEP_COLS = 2 * P

RAW_RING, X_RING, Y_RING = 4, 2, 8
R_RING, HL_RING = 3, 2


def pair_index(i, j):
    return i * (2 * FIELDS - i - 1) // 2 + (j - i - 1)


def plan():
    steps, tiles = [], []
    for n in range(BLOCKS):
        if n % 2:
            steps.append(("diag", n, n, len(tiles)))
            tiles.append([(2 * n - 2, 2 * n - 1), (2 * n, 2 * n + 1)])
        for m in range(n):
            steps.append(("full", n, m, len(tiles)))
            tiles.append([(2 * m, 2 * n), (2 * m + 1, 2 * n)])
            tiles.append([(2 * m, 2 * n + 1), (2 * m + 1, 2 * n + 1)])
    return steps, tiles


STEPS, TILES = plan()
NSTEPS, NTILES = len(STEPS), len(TILES)
CHUNKS = NSTEPS // CHUNK
QUADS = -(-NTILES // QUAD)
GROUPS = -(-NTILES // GROUP)
DENSE_ROW = P - DENSE
SEL = 32 - 2
assert NSTEPS % CHUNK == 0


def z_row(q):
    return q // GROUP, 32 * (q % QUAD) + 2 * ((q % GROUP) // QUAD)


def sum_place(i):
    return QUAD * (i // HALVES) + QUAD + 1 + 2 * (i % HALVES)


AHEAD = 4
def turn_steps():
    first = [next((s for s, x in enumerate(STEPS) if x[1] == n), 0) for n in range(BLOCKS)]
    out = [0, 0]
    for n in range(2, BLOCKS):
        ahead = 0 if n <= 5 else 2 if n < 8 else AHEAD
        out.append(first[n] - ahead)
    return out


TURN = turn_steps()


def split_plan():
    out = [([], [], []) for _ in range(NSTEPS)]
    for n in range(BLOCKS):
        first = next((s for s, q in enumerate(STEPS) if q[1] == n), 0)
        for i in range(4):
            piece = (n, i // 2, i % 2)
            s = TURN[n] + LATER + i // 2
            if n < 2:
                out[0][0].append(piece)
            elif n >= SPREAD and s < first and STEPS[s][0] == "full":
                out[s][1 + i % 2].append(piece)
            else:
                out[min(s, first) if n >= SPREAD else TURN[n]][1].append(piece)
    return out


LATER, SPREAD = 1, 8
SPLITS = split_plan()
K_POOL = 12
CALM = 36
PER_STEP = 2


def gather_plan():
    out = [[] for _ in range(NSTEPS)]
    units = [(n, t, f) for n in range(RAW_RING, BLOCKS) for t in range(BTILES) for f in range(2)]
    for s in range(NSTEPS):
        while units and TURN[units[0][0] - RAW_RING] <= s and (s < CALM or len(out[s]) < PER_STEP):
            out[s].append(units.pop(0))
    assert not units
    for s, us in enumerate(out):
        assert all(s < TURN[n] or s < CALM for n, _, _ in us)
    return out


GATHERS = gather_plan()


def build(nc, dense_t, ids, tables, w1, b1, w2, b2, w3, kstream, consts, out):
    F32, F32R, I32 = mybir.dt.float32, mybir.dt.float32r, mybir.dt.int32
    ALU, ACT = mybir.AluOpType, mybir.ActivationFunctionType

    with ExitStack() as ctx:
        def sb(name, shape, dt=F32):
            return ctx.enter_context(nc.sbuf_tensor(name, shape, dt))

        def sem(name):
            return ctx.enter_context(nc.semaphore(name))

        cst = sb("cst", [P, P + SEL + 32])
        ident = cst[:, 0:P]
        sel = cst[:, P:P + SEL + 32]
        idx = sb("idx", [P, BTILES, FIELDS], I32)
        raw = sb("raw", [P, RAW_RING, BTILES, P])
        emb = sb("emb", [P, BLOCKS, BATCH])
        diag_emb = sb("diag_emb", [P, BATCH])
        x = sb("x", [P, X_RING, 2, BATCH], F32R)
        k_raw = sb("k_raw", [P, R_RING, CHUNK, STEP_COLS])
        k_hi = sb("k_hi", [P, HL_RING, CHUNK, STEP_COLS], F32R)
        k_lo = sb("k_lo", [P, HL_RING, CHUNK, STEP_COLS], F32R)
        y = sb("y", [P, Y_RING, BATCH])
        z = sb("z", [P, GROUPS, BATCH])
        w3_sb = sb("w3_sb", [P, HID2 // P])
        b1_sb = sb("b1_sb", [P, HID1 // P])
        b2_sb = sb("b2_sb", [P, HID2 // P])
        out_sb = y[0:1, 0, :]
        w1_sb = raw[:, :, :, :].rearrange("p r t c -> p (r t c)")[:, 0:GROUPS * HID1].rearrange(
            "p (g n) -> p g n", g=GROUPS)
        w2_sb = emb[:, BLOCKS - 1, :].rearrange("p (k n) -> p k n", n=HID2)
        h1 = emb[:, 0:HID1 // P, :]
        h2 = emb[:, HID1 // P:HID1 // P + HID2 // P, :]

        prod = [ctx.enter_context(nc.psum_tensor(f"prod{i}", [P, BATCH], F32)) for i in range(2)]
        zsum = ctx.enter_context(nc.psum_tensor("zsum", [P, BATCH], F32))
        turned = ctx.enter_context(nc.psum_tensor("turned", [P, BATCH], F32))

        idx_in = sem("idx_in")
        const_in = sem("const_in")
        small_in = sem("small_in")
        w1_in = sem("w1_in")
        w2_in = sem("w2_in")
        gathered = [sem(f"gathered{i}") for i in range(RAW_RING)]
        k_in = [sem(f"k_in{i}") for i in range(R_RING)]
        khi_ready = sem("khi_ready")
        klo_ready = sem("klo_ready")
        block_turned = sem("block_turned")
        emb_ready = sem("emb_ready")
        block_saved = sem("block_saved")
        xhi_ready = sem("xhi_ready")
        xlo_ready = sem("xlo_ready")
        prod_ready = sem("prod_ready")
        y_ready = sem("y_ready")
        half_summed = sem("half_summed")
        z_saved = sem("z_saved")
        h_acc = sem("h_acc")
        h_ready = sem("h_ready")
        out_done = sem("out_done")

        def steps_tiles(s):
            return STEPS[s][3] if s < NSTEPS else NTILES

        def tiles_before_block(n):
            return next((STEPS[s][3] for s in range(NSTEPS) if STEPS[s][1] >= n), NTILES)

        block = ctx.enter_context(nc.Block())

        @block.sync
        def _(sp):
            sp.dma_start(idx[:, :, :], ids.rearrange("(t p) f -> p t f", p=P)).then_inc(idx_in, 16)
            sp.dma_start(cst[:, :], consts).then_inc(const_in, 16)
            for c in range(CHUNKS):
                if c >= R_RING:
                    sp.wait_ge(klo_ready, c - R_RING + 1)
                for h in range(2):
                    sp.dma_start(k_raw[64 * h:64 * h + 64, c % R_RING, :, :],
                                 kstream[:, c, :, :]).then_inc(k_in[c % R_RING], 16)
                if c == 2:
                    sp.dma_start(z[DENSE_ROW:P, GROUPS - 1, :], dense_t).then_inc(small_in, 16)
                    sp.dma_start(w3_sb[:, :], w3).then_inc(small_in, 16)
                    sp.dma_start(b1_sb[:, :], b1).then_inc(small_in, 16)
                    sp.dma_start(b2_sb[:, :], b2).then_inc(small_in, 16)
            sp.wait_ge(block_turned, BLOCKS)
            sp.dma_start(w1_sb, w1).then_inc(w1_in, 16)
            sp.wait_ge(xlo_ready, 4 * BLOCKS)
            sp.dma_start(w2_sb, w2).then_inc(w2_in, 16)
            sp.wait_ge(h_ready, 2 * (HID1 // P + HID2 // P) + HALVES)
            sp.dma_start(out, out_sb).then_inc(out_done, 16)
            sp.wait_ge(out_done, 16)

        def split_weights(eng, c):
            eng.wait_ge(khi_ready, c + 1)
            eng.tensor_tensor(k_lo[:, c % HL_RING, :, :], k_raw[:, c % R_RING, :, :],
                              k_hi[:, c % HL_RING, :, :].bitcast(F32), ALU.subtract).then_inc(klo_ready, 1)

        def split_block(n, f, h):
            a, b = slice(64 * f, 64 * f + 64), slice(64 - 64 * f, 128 - 64 * f)
            cols = slice(HALF * h, HALF * (h + 1))
            nc.vector.wait_ge(emb_ready, n + 1)
            nc.vector.wait_ge(xhi_ready, 2 * n + f + 1)
            nc.vector.tensor_tensor(x[b, n % X_RING, f, cols], emb[a, n, cols],
                                    x[a, n % X_RING, f, cols].bitcast(F32), ALU.subtract).then_inc(xlo_ready, 1)

        @block.gpsimd
        def _(pool):
            def gather(n, t, f):
                pool.indirect_dma_start(
                    raw[:, n % RAW_RING, t, EMBED * f:EMBED * (f + 1)], None, tables[2 * n + f],
                    bass.IndirectOffsetOnAxis(ap=idx[:, t, 2 * n + f:2 * n + f + 1], axis=0),
                ).then_inc(gathered[n % RAW_RING], 16)

            pool.wait_ge(idx_in, 16)
            for n in range(RAW_RING):
                for t in range(BTILES):
                    for f in range(2):
                        gather(n, t, f)
            for s in range(NSTEPS):
                c = s // CHUNK + 1
                if s % CHUNK == 2 and max(2, K_POOL) <= c < CHUNKS:
                    split_weights(pool, c)
                for n, t, f in GATHERS[s]:
                    if (t, f) == (0, 0):
                        pool.wait_ge(block_turned, n - RAW_RING + 1)
                    gather(n, t, f)

        @block.tensor
        def _(pe):
            pe.wait_ge(const_in, 16)

            def turn(n):
                pe.wait_ge(gathered[n % RAW_RING], 16 * 2 * BTILES * (n // RAW_RING + 1))
                if n:
                    pe.wait_ge(block_saved, n)
                for t in range(BTILES):
                    last = pe.transpose(turned[:, P * t:P * (t + 1)], raw[:, n % RAW_RING, t, :], ident)
                last.then_inc(block_turned, 1)

            def product(q, passes):
                if q >= 2:
                    pe.wait_ge(y_ready, q - 1)
                acc = prod[q % 2]
                for i, (w, mov) in enumerate(passes):
                    for h in range(HALVES):
                        last = pe.matmul(acc[:, HALF * h:HALF * (h + 1)], w, mov[:, HALF * h:HALF * (h + 1)],
                                         start=(i == 0), stop=(i == len(passes) - 1))
                last.then_inc(prod_ready, 1)

            def reduce_quad(k, h):
                tiles = range(QUAD * k, min(QUAD * (k + 1), NTILES))
                g, slot = QUAD * k // GROUP, (QUAD * k % GROUP) // QUAD
                if slot == 0 and g:
                    pe.wait_ge(z_saved, HALVES * (g - 1) + h + 1)
                pe.wait_ge(y_ready, tiles[-1] + 1)
                for q in tiles:
                    c = 32 * (q % QUAD)
                    last = pe.matmul(zsum[c:c + 32, HALF * h:HALF * (h + 1)],
                                     sel[:, SEL - 2 * slot:SEL - 2 * slot + 32],
                                     y[:, q % Y_RING, HALF * h:HALF * (h + 1)],
                                     start=(slot == 0), stop=(q + QUAD >= min(NTILES, GROUP * (g + 1))),
                                     tile_position=(0, c))
                last.then_inc(half_summed, 1)

            def reduce_due(q, sums):
                while sum_place(sums) == q:
                    reduce_quad(sums // HALVES, sums % HALVES)
                    sums += 1
                return sums

            turn(0)
            turn(1)
            sums = 0
            for s, (kind, n, m, q) in enumerate(STEPS):
                for nn in range(2, BLOCKS):
                    if TURN[nn] == s:
                        turn(nn)
                c = s // CHUNK
                if s % CHUNK == 0:
                    pe.wait_ge(klo_ready, c + 1)
                if s == 0 or STEPS[s - 1][1] != n:
                    pe.wait_ge(xlo_ready, 4 * (n + 1))
                hi, lo = (k[:, c % HL_RING, s % CHUNK, :] for k in (k_hi, k_lo))
                if kind == "full":
                    for f in range(2):
                        cols = slice(P * f, P * (f + 1))
                        mov = x[:, n % X_RING, f, :]
                        product(q + f, [(hi[:, cols], mov), (lo[:, cols], mov)])
                        sums = reduce_due(q + f, sums)
                else:
                    passes = []
                    for f in range(2):
                        cols = slice(P * f, P * (f + 1))
                        mov = x[:, (n - 1 + f) % X_RING, 1, :]
                        passes += [(hi[:, cols], mov), (lo[:, cols], mov)]
                    product(q, passes)
                    sums = reduce_due(q, sums)
            while sums < HALVES * QUADS:
                reduce_quad(sums // HALVES, sums % HALVES)
                sums += 1

            pe.wait_ge(small_in, 16 * 4)
            pe.wait_ge(w1_in, 16)
            pe.wait_ge(w2_in, 16)
            banks = [prod[0][:, 0:HALF], prod[0][:, HALF:], prod[1][:, 0:HALF], prod[1][:, HALF:]]
            accs = 0

            def layer(w, src, rows, h, k_tiles, out_rows, need):
                nonlocal accs
                pe.wait_ge(*need)
                if accs >= 4:
                    pe.wait_ge(h_ready, accs - 3)
                for k in range(k_tiles):
                    last = pe.matmul(banks[accs % 4][0:out_rows, :], w[:, k, rows],
                                     src[:, k, HALF * h:HALF * (h + 1)], start=(k == 0), stop=(k == k_tiles - 1))
                last.then_inc(h_acc, 1)
                accs += 1

            for h in range(HALVES):
                for m in range(HID1 // P):
                    layer(w1_sb, z, slice(P * m, P * (m + 1)), h, GROUPS, P, (z_saved, HALVES * (GROUPS - 1) + h + 1))
            for h in range(HALVES):
                for m in range(HID2 // P):
                    layer(w2_sb, h1, slice(P * m, P * (m + 1)), h, HID1 // P, P, (h_ready, HID1 // P * (h + 1)))
            w3_v = w3_sb[:, :].rearrange("p (k o) -> p k o", o=1)
            for h in range(HALVES):
                layer(w3_v, h2, slice(0, 1), h, HID2 // P, 1, (h_ready, 2 * HID1 // P + HID2 // P * (h + 1)))

        @block.scalar
        def _(act):
            def split_k(c):
                act.wait_ge(k_in[c % R_RING], 32 * (c // R_RING + 1))
                if c >= HL_RING:
                    act.wait_ge(prod_ready, steps_tiles(CHUNK * (c - HL_RING + 1)))
                act.copy(k_hi[:, c % HL_RING, :, :], k_raw[:, c % R_RING, :, :]).then_inc(khi_ready, 1)

            def save_block(n):
                act.wait_ge(block_turned, n + 1)
                if n >= X_RING:
                    act.wait_ge(prod_ready, tiles_before_block(n - 1) + (n % 2 == 0))
                act.copy(emb[:, n, :], turned[:, :]).then_inc(emb_ready, 1)
                for f in range(2):
                    rows = slice(64 * f, 64 * f + 64)
                    act.copy(x[rows, n % X_RING, f, :], turned[rows, :]).then_inc(xhi_ready, 1)
                r = slice(64 * (n % 2), 64 * (n % 2) + 64)
                if n >= 2 and n % 2 == 0:
                    act.wait_ge(y_ready, tiles_before_block(n - 1) + 1)
                act.copy(diag_emb[r, :], turned[0:64, :]).then_inc(block_saved, 1)

            def last_sum(i):
                return HALVES * (min(GROUP // QUAD * (i // HALVES + 1), QUADS) - 1) + i % HALVES

            def save_z(i):
                g, h = i // HALVES, slice(HALF * (i % HALVES), HALF * (i % HALVES + 1))
                act.wait_ge(half_summed, last_sum(i) + 1)
                rows = P if g < GROUPS - 1 else DENSE_ROW
                act.copy(z[0:rows, g, h], zsum[0:rows, h]).then_inc(z_saved, 1)

            split_k(0)
            split_k(1)
            save_block(0)
            save_block(1)
            groups = 0
            for s in range(NSTEPS):
                if s % CHUNK == 2 and s // CHUNK + 1 >= 2 and s // CHUNK + 1 < CHUNKS:
                    split_k(s // CHUNK + 1)
                for nn in range(2, BLOCKS):
                    if TURN[nn] == s:
                        save_block(nn)
                while groups < HALVES * GROUPS and sum_place(last_sum(groups)) < steps_tiles(s + 1):
                    save_z(groups)
                    groups += 1
            while groups < HALVES * GROUPS:
                save_z(groups)
                groups += 1

            banks = [prod[0][:, 0:HALF], prod[0][:, HALF:], prod[1][:, 0:HALF], prod[1][:, HALF:]]
            accs = 0
            for dst, bias, mtiles in ((h1, b1_sb, HID1 // P), (h2, b2_sb, HID2 // P)):
                for h in range(HALVES):
                    for m in range(mtiles):
                        act.wait_ge(h_acc, accs + 1)
                        act.activation(dst[:, m, HALF * h:HALF * (h + 1)], banks[accs % 4], ACT.Relu,
                                       bias=bias[:, m:m + 1]).then_inc(h_ready, 1)
                        accs += 1
            for h in range(HALVES):
                act.wait_ge(h_acc, accs + 1)
                act.copy(out_sb[:, HALF * h:HALF * (h + 1)], banks[accs % 4][0:1, :]).then_inc(h_ready, 1)
                accs += 1

        @block.vector
        def _(dve):
            def multiply(q, e):
                dve.wait_ge(prod_ready, q + 1)
                if q >= Y_RING:
                    dve.wait_ge(half_summed, HALVES * ((q - Y_RING) // QUAD + 1))
                dve.tensor_tensor(y[:, q % Y_RING, :], prod[q % 2][:, :], e, ALU.mult).then_inc(y_ready, 1)

            split_weights(dve, 0)
            split_weights(dve, 1)
            for n, f, h in SPLITS[0][0]:
                split_block(n, f, h)
            for s, (kind, n, m, q) in enumerate(STEPS):
                c = s // CHUNK + 1
                if s % CHUNK == 2 and 2 <= c < min(K_POOL, CHUNKS):
                    split_weights(dve, c)
                for piece in SPLITS[s][1]:
                    split_block(*piece)
                if kind == "full":
                    dve.wait_ge(emb_ready, m + 1)
                    for f in range(2):
                        if f:
                            for piece in SPLITS[s][2]:
                                split_block(*piece)
                        multiply(q + f, emb[:, m, :])
                else:
                    dve.wait_ge(block_saved, n + 1)
                    multiply(q, diag_emb[:, :])


def kernel(**inputs):
    import concourse.bacc as bacc
    from concourse.bass_utils import run_bass_kernel_spmd

    a = {k: np.asarray(v) for k, v in inputs.items()}
    K = a["L0_rec_kernel"]
    kstream = np.zeros((EMBED, NSTEPS, 2, 2, EMBED), K.dtype)
    for s, (kind, n, m, q) in enumerate(STEPS):
        if kind == "full":
            for f in range(2):
                for r in range(2):
                    kstream[:, s, f, r] = K[:, pair_index(*TILES[q + f][r])]
        else:
            for f in range(2):
                kstream[:, s, f, f] = K[:, pair_index(*TILES[q][f])]
    kstream = kstream.reshape(EMBED, CHUNKS, CHUNK, STEP_COLS)
    W1 = a["W_top1"]
    w1 = np.zeros((P, GROUPS, HID1), W1.dtype)
    for q, pairs in enumerate(TILES):
        g, row = z_row(q)
        for r in range(2):
            w1[row + r, g] = W1[pair_index(*pairs[r])]
    w1[DENSE_ROW:, GROUPS - 1] = W1[-DENSE:]
    consts = np.zeros((P, P + SEL + 32), np.float32)
    consts[:, 0:P] = np.eye(P, dtype=np.float32)
    for r in range(2):
        consts[64 * r:64 * r + 64, P + SEL + r] = 1.0

    def chunks(w, n):
        return np.ascontiguousarray(w.reshape(n, P, -1).transpose(1, 0, 2))

    arrays = {
        "dense_t": np.ascontiguousarray(a["dense_ctx"].T),
        "ids": a["ids"],
        "w1": w1,
        "b1": np.ascontiguousarray(a["b_top1"].reshape(-1, P).T),
        "w2": chunks(a["W_top2"], HID1 // P),
        "b2": np.ascontiguousarray(a["b_top2"].reshape(-1, P).T),
        "w3": np.ascontiguousarray(a["W_top3"].reshape(-1, P).T),
        "kstream": kstream,
        "consts": consts,
    }
    for f in range(FIELDS):
        arrays[f"tbl_{f}"] = a[f"tbl_{f}"]
    nc = bacc.Bacc("TRN2", target_bir_lowering=False, num_devices=1)
    h = {k: nc.dram_tensor(k, v.shape, mybir.dt.from_np(v.dtype), kind="ExternalInput").ap()
         for k, v in arrays.items()}
    out = nc.dram_tensor("out", (BATCH, 1), mybir.dt.float32, kind="ExternalOutput").ap()
    build(nc, h["dense_t"], h["ids"], [h[f"tbl_{f}"] for f in range(FIELDS)], h["w1"], h["b1"], h["w2"],
          h["b2"], h["w3"], h["kstream"], h["consts"], out.rearrange("b o -> o b"))
    got = run_bass_kernel_spmd(nc, [arrays], core_ids=[0])
    return got.results[0]["out"]
```

```python
from contextlib import ExitStack

import numpy as np

import concourse.bass as bass
from concourse import mybir

P = 128
FIELDS, EMBED, BATCH = 40, 64, 1024
DENSE, HID1, HID2 = 16, 512, 256
BLOCKS = FIELDS // 2
HALF = 512
HALVES = BATCH // HALF
BTILES = BATCH // P
QUAD = 4
GROUP = 16 * QUAD
CHUNK = 2
STEP_COLS = 2 * P

TABLE_ROWS = [1250, 1250, 1250, 1000, 125000, 125000, 1250, 125000, 1250, 12500, 12500, 1250, 12500, 1000,
              12500, 12500, 12500, 1000, 12500, 1000, 1250, 1000, 1250, 1250, 1250, 1250, 1250, 1000, 1250,
              1250, 1000, 1250, 1250, 1250, 1000, 1250, 1250, 1000, 1000, 1000]
HOT_BLOCKS = 2
HOT_FIELDS = 2 * HOT_BLOCKS
HOT_TILES = -(-min(TABLE_ROWS) // P)
SMALL = [f for f in range(FIELDS) if TABLE_ROWS[f] <= HOT_TILES * P][:HOT_FIELDS]
ORDER = SMALL + [f for f in range(FIELDS) if f not in SMALL]

RAW_RING, X_RING, Y_RING = 4, 3, 8
R_RING, HL_RING = 2, 3


def pair_index(i, j):
    return i * (2 * FIELDS - i - 1) // 2 + (j - i - 1)


def plan():
    steps, tiles = [], []
    for n in range(BLOCKS):
        if n % 2:
            steps.append(("diag", n, n, len(tiles)))
            tiles.append([(2 * n - 2, 2 * n - 1), (2 * n, 2 * n + 1)])
        for m in range(n):
            steps.append(("full", n, m, len(tiles)))
            tiles.append([(2 * m, 2 * n), (2 * m + 1, 2 * n)])
            tiles.append([(2 * m, 2 * n + 1), (2 * m + 1, 2 * n + 1)])
    return steps, tiles


STEPS, TILES = plan()
NSTEPS, NTILES = len(STEPS), len(TILES)
CHUNKS = NSTEPS // CHUNK
QUADS = -(-NTILES // QUAD)
GROUPS = -(-NTILES // GROUP)
DENSE_ROW = P - DENSE
SEL = 32 - 2
assert NSTEPS % CHUNK == 0


def z_row(q):
    return q // GROUP, 32 * (q % QUAD) + 2 * ((q % GROUP) // QUAD)


def sum_place(i):
    return QUAD * (i // HALVES) + QUAD + 1 + 2 * (i % HALVES)


EARLY = [1, 2, 2, 2, 4, 5, 4, 3, 2]
AHEAD = 3
LO_LATER = 1
SPLIT_LATER = 1
K_STEP = 0
X_POOL = 11
K_POOL = 28
CALM, PER_STEP = 36, 2

FIRST = [next((s for s, x in enumerate(STEPS) if x[1] == n), 0) for n in range(BLOCKS)]
TURN = [0] * HOT_BLOCKS + [FIRST[n] - (EARLY + [AHEAD] * BLOCKS)[n - HOT_BLOCKS] for n in range(HOT_BLOCKS, BLOCKS)]
LOW_AT = [min(TURN[n] + LO_LATER, FIRST[n]) for n in range(BLOCKS)]
DIAG_AT = [FIRST[n] if n % 2 == 0 else max(LOW_AT[n], FIRST[n - 1] + 1) for n in range(BLOCKS)]
SPLIT_AT = [min(STEPS[TURN[n]][3] + SPLIT_LATER, STEPS[FIRST[n]][3]) for n in range(BLOCKS)]


def gather_plan():
    out = [[] for _ in range(NSTEPS)]
    units = [(n, t, f) for n in range(HOT_BLOCKS + RAW_RING, BLOCKS) for t in range(BTILES) for f in range(2)]
    for s in range(NSTEPS):
        while units and TURN[units[0][0] - RAW_RING] <= s and (s < CALM or len(out[s]) < PER_STEP):
            out[s].append(units.pop(0))
    assert not units and all(s < TURN[n] or s < CALM for s, us in enumerate(out) for n, _, _ in us)
    return out


GATHERS = gather_plan()


def build(nc, dense_t, ids, hot_ids, hot_tables, tables, w1, b1, w2, b2, w3, kstream, consts, out):
    F32, F32R, I32 = mybir.dt.float32, mybir.dt.float32r, mybir.dt.int32
    ALU, ACT = mybir.AluOpType, mybir.ActivationFunctionType

    with ExitStack() as ctx:
        def sb(name, shape, dt=F32):
            return ctx.enter_context(nc.sbuf_tensor(name, shape, dt))

        def sem(name):
            return ctx.enter_context(nc.semaphore(name))

        cst = sb("cst", [P, P + SEL + 32 + HOT_TILES])
        ident = cst[:, 0:P]
        sel = cst[:, P:P + SEL + 32]
        hot_row = cst[:, P + SEL + 32:]
        idx = sb("idx", [P, BTILES, FIELDS], I32)
        raw = sb("raw", [P, RAW_RING, BTILES, P])
        emb = sb("emb", [P, BLOCKS, BATCH])
        diag_emb = sb("diag_emb", [P, BATCH])
        x = sb("x", [P, X_RING, 2, BATCH], F32R)
        low = sb("low", [P, BATCH], F32R)
        k_raw = sb("k_raw", [P, R_RING, CHUNK, STEP_COLS])
        k_hi = sb("k_hi", [P, HL_RING, CHUNK, STEP_COLS], F32R)
        k_lo = sb("k_lo", [P, HL_RING, CHUNK, STEP_COLS], F32R)
        y = sb("y", [P, Y_RING, BATCH])
        with ExitStack() as early:
            def hot(name, shape, dt=F32):
                return early.enter_context(nc.sbuf_tensor(name, shape, dt))

            hot_raw = hot("hot_raw", [P, 2, HOT_TILES, EMBED])
            hot_idx = hot("hot_idx", [P, 2, BATCH], I32)
            hot_w = hot("hot_w", [P, 2, HOT_TILES, 2 * EMBED], F32R)
            onehot = hot("onehot", [P, 2, BATCH], F32R)
        z = sb("z", [P, GROUPS, BATCH])
        w3_sb = sb("w3_sb", [P, HID2 // P])
        b1_sb = sb("b1_sb", [P, HID1 // P])
        b2_sb = sb("b2_sb", [P, HID2 // P])
        out_sb = y[0:1, 0, :]
        w1_sb = raw[:, :, :, :].rearrange("p r t c -> p (r t c)")[:, 0:GROUPS * HID1].rearrange(
            "p (g n) -> p g n", g=GROUPS)
        w2_sb = emb[:, BLOCKS - 1, :].rearrange("p (k n) -> p k n", n=HID2)
        h1 = emb[:, 0:HID1 // P, :]
        h2 = emb[:, HID1 // P:HID1 // P + HID2 // P, :]

        prod = [ctx.enter_context(nc.psum_tensor(f"prod{i}", [P, BATCH], F32)) for i in range(2)]
        zsum = ctx.enter_context(nc.psum_tensor("zsum", [P, BATCH], F32))
        turned = ctx.enter_context(nc.psum_tensor("turned", [P, BATCH], F32))

        idx_in = sem("idx_in")
        const_in = sem("const_in")
        small_in = sem("small_in")
        w1_in = sem("w1_in")
        w2_in = sem("w2_in")
        gathered = [sem(f"gathered{i}") for i in range(RAW_RING)]
        hot_in = [sem(f"hot_in{i}") for i in range(2)]
        k_in = [sem(f"k_in{i}") for i in range(R_RING)]
        out_done = sem("out_done")
        hot_hi = sem("hot_hi")
        hot_lo = sem("hot_lo")
        onehot_ready = sem("onehot_ready")
        onehot_used = sem("onehot_used")
        hot_low_saved = sem("hot_low_saved")
        hot_summed = sem("hot_summed")
        looked = [turned, prod[0], prod[1]]
        khi_ready = sem("khi_ready")
        klo_ready = sem("klo_ready")
        block_turned = sem("block_turned")
        emb_ready = sem("emb_ready")
        high_ready = sem("high_ready")
        low_ready = sem("low_ready")
        xlo_ready = sem("xlo_ready")
        xhi_ready = sem("xhi_ready")
        diag_saved = sem("diag_saved")
        prod_ready = sem("prod_ready")
        y_ready = sem("y_ready")
        half_summed = sem("half_summed")
        z_saved = sem("z_saved")
        h_acc = sem("h_acc")
        h_ready = sem("h_ready")

        def steps_tiles(s):
            return STEPS[s][3] if s < NSTEPS else NTILES

        def tiles_before_block(n):
            return next((STEPS[s][3] for s in range(NSTEPS) if STEPS[s][1] >= n), NTILES)

        block = ctx.enter_context(nc.Block())

        @block.sync
        def _(sp):
            sp.dma_start(idx[:, :, :], ids.rearrange("(t p) f -> p t f", p=P)).then_inc(idx_in, 16)

            def load_hot(f):
                if f >= 2:
                    sp.wait_ge(onehot_ready, HOT_TILES * (f - 1))
                sp.dma_start(hot_raw[:, f % 2, :, :], hot_tables[f]).then_inc(hot_in[f % 2], 16)
                sp.dma_start(hot_idx[:, f % 2, :], hot_ids[f, :].partition_broadcast(P)).then_inc(hot_in[f % 2], 16)

            load_hot(0)
            sp.dma_start(cst[:, :], consts).then_inc(const_in, 16)
            load_hot(1)

            def load_weights(c, slot):
                for h in range(2):
                    sp.dma_start(k_raw[64 * h:64 * h + 64, slot, :, :],
                                 kstream[:, bass.ds(c, 1), :, :].rearrange("e o s n -> e (o s) n")
                                 ).then_inc(k_in[slot], 16)

            for c in range(R_RING):
                load_weights(c, c)
            for f in range(2, HOT_FIELDS):
                load_hot(f)
            sp.dma_start(w3_sb[:, :], w3).then_inc(small_in, 16)
            sp.dma_start(b1_sb[:, :], b1).then_inc(small_in, 16)
            sp.dma_start(b2_sb[:, :], b2).then_inc(small_in, 16)
            with sp.Fori(1, CHUNKS // R_RING) as turns:
                for slot in range(R_RING):
                    c = turns * R_RING + slot
                    sp.wait_ge(klo_ready, c - R_RING + 1)
                    load_weights(c, slot)
            sp.wait_ge(block_turned, BLOCKS - HOT_BLOCKS)
            sp.dma_start(w1_sb, w1).then_inc(w1_in, 16)
            sp.dma_start(z[DENSE_ROW:P, GROUPS - 1, :], dense_t).then_inc(small_in, 16)
            sp.wait_ge(xlo_ready, 2 * (BLOCKS - HOT_BLOCKS))
            sp.dma_start(w2_sb, w2).then_inc(w2_in, 16)
            sp.wait_ge(h_ready, 2 * (HID1 // P + HID2 // P) + HALVES)
            sp.dma_start(out, out_sb).then_inc(out_done, 16)
            sp.wait_ge(out_done, 16)

        def split_weights(eng, c):
            if c == K_POOL:
                eng.wait_ge(klo_ready, c)
            eng.wait_ge(khi_ready, c + 1)
            eng.tensor_tensor(k_lo[:, c % HL_RING, :, :], k_raw[:, c % R_RING, :, :],
                              k_hi[:, c % HL_RING, :, :].bitcast(F32), ALU.subtract).then_inc(klo_ready, 1)

        def split_block(eng, n):
            eng.wait_ge(emb_ready, n + 1 - HOT_BLOCKS)
            eng.wait_ge(high_ready, n + 1 - HOT_BLOCKS)
            eng.tensor_tensor(low[:, :], emb[:, n, :], low[:, :].bitcast(F32), ALU.subtract).then_inc(low_ready, 1)

        @block.gpsimd
        def _(pool):
            def gather(n, t, f):
                field = ORDER[2 * n + f]
                pool.indirect_dma_start(
                    raw[:, (n - HOT_BLOCKS) % RAW_RING, t, EMBED * f:EMBED * (f + 1)], None, tables[field],
                    bass.IndirectOffsetOnAxis(ap=idx[:, t, field:field + 1], axis=0),
                ).then_inc(gathered[(n - HOT_BLOCKS) % RAW_RING], 16)

            pool.wait_ge(idx_in, 16)
            for n in range(HOT_BLOCKS, HOT_BLOCKS + RAW_RING):
                for t in range(BTILES):
                    for f in range(2):
                        gather(n, t, f)
            for s in range(NSTEPS):
                c = s // CHUNK + HL_RING - 1
                if s % CHUNK == K_STEP and K_POOL <= c < CHUNKS:
                    split_weights(pool, c)
                for nn in range(X_POOL, BLOCKS):
                    if TURN[nn] == s:
                        split_block(pool, nn)
                for n, t, f in GATHERS[s]:
                    if (t, f) == (0, 0):
                        pool.wait_ge(block_turned, n + 1 - HOT_BLOCKS - RAW_RING)
                    gather(n, t, f)

        @block.tensor
        def _(pe):
            pe.wait_ge(const_in, 16)

            def turn(n):
                slot, turn_no = (n - HOT_BLOCKS) % RAW_RING, (n - HOT_BLOCKS) // RAW_RING
                pe.wait_ge(gathered[slot], 16 * 2 * BTILES * (turn_no + 1))
                if n == HOT_BLOCKS:
                    pe.wait_ge(hot_summed, HOT_FIELDS)
                else:
                    pe.wait_ge(xhi_ready, 2 * n)
                for t in range(BTILES):
                    last = pe.transpose(turned[:, P * t:P * (t + 1)], raw[:, slot, t, :], ident)
                last.then_inc(block_turned, 1)

            def look_up(n):
                for i in range(2 * n, 2 * n + 2):
                    if i >= len(looked):
                        pe.wait_ge(hot_summed, i + 1 - len(looked))
                    pe.wait_ge(hot_lo, i + 1)
                    for t in range(HOT_TILES):
                        pe.wait_ge(onehot_ready, HOT_TILES * i + t + 1)
                        for h in range(HALVES):
                            cols = slice(HALF * h, HALF * (h + 1))
                            last = pe.matmul(looked[i % 3][:, cols], hot_w[:, i % 2, t, :], onehot[:, t % 2, cols],
                                             start=(t == 0), stop=(t == HOT_TILES - 1))
                        last.then_inc(onehot_used, 1)

            def product(q, passes):
                if q >= 2:
                    pe.wait_ge(y_ready, q - 1)
                acc = prod[q % 2]
                for i, (w, mov) in enumerate(passes):
                    for h in range(HALVES):
                        last = pe.matmul(acc[:, HALF * h:HALF * (h + 1)], w, mov[:, HALF * h:HALF * (h + 1)],
                                         start=(i == 0), stop=(i == len(passes) - 1))
                last.then_inc(prod_ready, 1)

            def reduce_quad(k, h):
                tiles = range(QUAD * k, min(QUAD * (k + 1), NTILES))
                g, slot = QUAD * k // GROUP, (QUAD * k % GROUP) // QUAD
                if slot == 0 and g:
                    pe.wait_ge(z_saved, HALVES * (g - 1) + h + 1)
                pe.wait_ge(y_ready, tiles[-1] + 1)
                for q in tiles:
                    c = 32 * (q % QUAD)
                    last = pe.matmul(zsum[c:c + 32, HALF * h:HALF * (h + 1)],
                                     sel[:, SEL - 2 * slot:SEL - 2 * slot + 32],
                                     y[:, q % Y_RING, HALF * h:HALF * (h + 1)],
                                     start=(slot == 0), stop=(q + QUAD >= min(NTILES, GROUP * (g + 1))),
                                     tile_position=(0, c))
                last.then_inc(half_summed, 1)

            def reduce_due(q, sums):
                while sum_place(sums) == q:
                    reduce_quad(sums // HALVES, sums % HALVES)
                    sums += 1
                return sums

            look_up(0)
            look_up(1)
            pe.wait_ge(hot_summed, HOT_FIELDS - 1)
            sums = 0
            for s, (kind, n, m, q) in enumerate(STEPS):
                for nn in range(2, BLOCKS):
                    if TURN[nn] == s:
                        turn(nn)
                c = s // CHUNK
                if s % CHUNK == 0:
                    pe.wait_ge(klo_ready, c + 1)
                if s == 0 or STEPS[s - 1][1] != n:
                    if n < HOT_BLOCKS:
                        pe.wait_ge(xhi_ready, 2 * (n + 1))
                    else:
                        pe.wait_ge(xlo_ready, 2 * (n - HOT_BLOCKS + 1))
                hi, lo = (k[:, c % HL_RING, s % CHUNK, :] for k in (k_hi, k_lo))
                if kind == "full":
                    for f in range(2):
                        cols = slice(P * f, P * (f + 1))
                        mov = x[:, n % X_RING, f, :]
                        product(q + f, [(hi[:, cols], mov), (lo[:, cols], mov)])
                        sums = reduce_due(q + f, sums)
                else:
                    passes = []
                    for f in range(2):
                        cols = slice(P * f, P * (f + 1))
                        mov = x[:, (n - 1 + f) % X_RING, 1, :]
                        passes += [(hi[:, cols], mov), (lo[:, cols], mov)]
                    product(q, passes)
                    sums = reduce_due(q, sums)
            while sums < HALVES * QUADS:
                reduce_quad(sums // HALVES, sums % HALVES)
                sums += 1

            pe.wait_ge(small_in, 16 * 4)
            pe.wait_ge(w1_in, 16)
            pe.wait_ge(w2_in, 16)
            banks = [prod[0][:, 0:HALF], prod[0][:, HALF:], prod[1][:, 0:HALF], prod[1][:, HALF:]]
            accs = 0

            def layer(w, src, rows, h, k_tiles, out_rows, need):
                nonlocal accs
                pe.wait_ge(*need)
                if accs >= 4:
                    pe.wait_ge(h_ready, accs - 3)
                for k in range(k_tiles):
                    if w is w1_sb and k == k_tiles - 1:
                        pe.wait_ge(z_saved, HALVES * (GROUPS - 1) + h + 1)
                    last = pe.matmul(banks[accs % 4][0:out_rows, :], w[:, k, rows],
                                     src[:, k, HALF * h:HALF * (h + 1)], start=(k == 0), stop=(k == k_tiles - 1))
                last.then_inc(h_acc, 1)
                accs += 1

            for h in range(HALVES):
                for m in range(HID1 // P):
                    layer(w1_sb, z, slice(P * m, P * (m + 1)), h, GROUPS, P, (z_saved, HALVES * (GROUPS - 1)))
            for h in range(HALVES):
                for m in range(HID2 // P):
                    layer(w2_sb, h1, slice(P * m, P * (m + 1)), h, HID1 // P, P, (h_ready, HID1 // P * (h + 1)))
            w3_v = w3_sb[:, :].rearrange("p (k o) -> p k o", o=1)
            for h in range(HALVES):
                layer(w3_v, h2, slice(0, 1), h, HID2 // P, 1, (h_ready, 2 * HID1 // P + HID2 // P * (h + 1)))

        @block.scalar
        def _(act):
            def split_k(c):
                act.wait_ge(k_in[c % R_RING], 32 * (c // R_RING + 1))
                if c >= HL_RING:
                    act.wait_ge(prod_ready, steps_tiles(CHUNK * (c - HL_RING + 1)))
                act.copy(k_hi[:, c % HL_RING, :, :], k_raw[:, c % R_RING, :, :]).then_inc(khi_ready, 1)

            def save_block(n):
                act.wait_ge(block_turned, n + 1 - HOT_BLOCKS)
                if n >= X_RING:
                    act.wait_ge(prod_ready, tiles_before_block(n - X_RING + 1) + ((n - X_RING) % 2 == 0))
                if n > HOT_BLOCKS:
                    act.wait_ge(xlo_ready, 2 * (n - HOT_BLOCKS))
                act.copy(low[:, :], turned[:, :]).then_inc(high_ready, 1)
                act.copy(emb[:, n, :], turned[:, :]).then_inc(emb_ready, 1)
                for f in range(2):
                    rows = slice(64 * f, 64 * f + 64)
                    act.copy(x[rows, n % X_RING, f, :], turned[rows, :]).then_inc(xhi_ready, 1)

            def save_diag(n):
                if n >= 2 and n % 2 == 0:
                    act.wait_ge(y_ready, tiles_before_block(n - 1) + 1)
                act.copy(diag_emb[64 * (n % 2):64 * (n % 2) + 64, :], emb[0:64, n, :]).then_inc(diag_saved, 1)

            def save_low(n):
                act.wait_ge(low_ready, n + 1 - HOT_BLOCKS)
                for f in range(2):
                    act.copy(x[64 - 64 * f:128 - 64 * f, n % X_RING, f, :],
                             low[64 * f:64 * f + 64, :].bitcast(F32)).then_inc(xlo_ready, 1)

            def last_sum(i):
                return HALVES * (min(GROUP // QUAD * (i // HALVES + 1), QUADS) - 1) + i % HALVES

            def save_z(i):
                g, h = i // HALVES, slice(HALF * (i % HALVES), HALF * (i % HALVES + 1))
                act.wait_ge(half_summed, last_sum(i) + 1)
                rows = P if g < GROUPS - 1 else DENSE_ROW
                act.copy(z[0:rows, g, h], zsum[0:rows, h]).then_inc(z_saved, 1)

            def split_hot(f):
                act.wait_ge(hot_in[f % 2], 32 * (f // 2 + 1))
                if f >= 2:
                    act.wait_ge(onehot_used, HOT_TILES * (f - 1))
                act.copy(hot_w[:, f % 2, :, 0:EMBED], hot_raw[:, f % 2, :, :]).then_inc(hot_hi, 1)

            def save_hot(n):
                for f in range(2):
                    i = 2 * n + f
                    rows = slice(64 * f, 64 * f + 64)
                    if 1 < i + 1 < HOT_FIELDS:
                        split_hot(i + 1)
                    act.wait_ge(onehot_used, HOT_TILES * (i + 1))
                    act.copy(x[:, n % X_RING, f, :], looked[i % 3][:, :]).then_inc(xhi_ready, 1)
                    act.copy(emb[rows, n, :], looked[i % 3][64:128, :]).then_inc(hot_low_saved, 1)

            split_hot(0)
            split_hot(1)
            save_hot(0)
            for c in range(HL_RING - 1):
                split_k(c)
            save_hot(1)
            for n in range(HOT_BLOCKS):
                act.wait_ge(hot_summed, 2 * n + 1)
                save_diag(n)
            groups = 0
            for s in range(NSTEPS):
                if s % CHUNK == K_STEP and s // CHUNK + HL_RING - 1 < CHUNKS:
                    split_k(s // CHUNK + HL_RING - 1)
                for nn in range(2, BLOCKS):
                    if TURN[nn] == s:
                        save_block(nn)
                    if LOW_AT[nn] == s:
                        save_low(nn)
                for nn in range(HOT_BLOCKS, BLOCKS):
                    if DIAG_AT[nn] == s:
                        save_diag(nn)
                while groups < HALVES * GROUPS and sum_place(last_sum(groups)) < steps_tiles(s + 1):
                    save_z(groups)
                    groups += 1
            while groups < HALVES * GROUPS:
                save_z(groups)
                groups += 1

            banks = [prod[0][:, 0:HALF], prod[0][:, HALF:], prod[1][:, 0:HALF], prod[1][:, HALF:]]
            accs = 0
            for dst, bias, mtiles in ((h1, b1_sb, HID1 // P), (h2, b2_sb, HID2 // P)):
                for h in range(HALVES):
                    for m in range(mtiles):
                        act.wait_ge(h_acc, accs + 1)
                        act.activation(dst[:, m, HALF * h:HALF * (h + 1)], banks[accs % 4], ACT.Relu,
                                       bias=bias[:, m:m + 1]).then_inc(h_ready, 1)
                        accs += 1
            for h in range(HALVES):
                act.wait_ge(h_acc, accs + 1)
                act.copy(out_sb[:, HALF * h:HALF * (h + 1)], banks[accs % 4][0:1, :]).then_inc(h_ready, 1)
                accs += 1

        @block.vector
        def _(dve):
            def splits_due(q):
                for nn in range(HOT_BLOCKS, X_POOL):
                    if SPLIT_AT[nn] == q:
                        split_block(dve, nn)

            def multiply(q, e):
                dve.wait_ge(prod_ready, q + 1)
                if q >= Y_RING:
                    dve.wait_ge(half_summed, HALVES * ((q - Y_RING) // QUAD + 1))
                dve.tensor_tensor(y[:, q % Y_RING, :], prod[q % 2][:, :], e, ALU.mult).then_inc(y_ready, 1)

            def add_hot(i):
                rows = slice(64 * (i % 2), 64 * (i % 2) + 64)
                dve.wait_ge(hot_low_saved, i + 1)
                dve.tensor_tensor(emb[rows, i // 2, :], looked[i % 3][0:64, :], emb[rows, i // 2, :],
                                  ALU.add).then_inc(hot_summed, 1)

            dve.wait_ge(const_in, 16)
            for i in range(HOT_FIELDS):
                dve.wait_ge(hot_hi, i + 1)
                dve.tensor_tensor(hot_w[:, i % 2, :, EMBED:], hot_raw[:, i % 2, :, :],
                                  hot_w[:, i % 2, :, 0:EMBED].bitcast(F32), ALU.subtract).then_inc(hot_lo, 1)
                for t in range(HOT_TILES):
                    if i and t == 5:
                        add_hot(i - 1)
                    if HOT_TILES * i + t >= 2:
                        dve.wait_ge(onehot_used, HOT_TILES * i + t - 1)
                    dve.tensor_scalar(onehot[:, t % 2, :], hot_idx[:, i % 2, :], hot_row[:, t:t + 1], None,
                                      ALU.is_equal).then_inc(onehot_ready, 1)
            for c in range(HL_RING - 1):
                split_weights(dve, c)
            add_hot(HOT_FIELDS - 1)
            for s, (kind, n, m, q) in enumerate(STEPS):
                c = s // CHUNK + HL_RING - 1
                if s % CHUNK == K_STEP and c < K_POOL:
                    split_weights(dve, c)
                if kind == "full":
                    if m < HOT_BLOCKS:
                        dve.wait_ge(hot_summed, 2 * m + 2)
                    else:
                        dve.wait_ge(emb_ready, m + 1 - HOT_BLOCKS)
                    for f in range(2):
                        splits_due(q + f)
                        multiply(q + f, emb[:, m, :])
                else:
                    splits_due(q)
                    dve.wait_ge(diag_saved, n + 1)
                    multiply(q, diag_emb[:, :])


def kernel(**inputs):
    import concourse.bacc as bacc
    from concourse.bass_utils import run_bass_kernel_spmd

    a = {k: np.asarray(v) for k, v in inputs.items()}
    K = a["L0_rec_kernel"]
    kstream = np.zeros((EMBED, NSTEPS, 2, 2, EMBED), K.dtype)

    def weights(i, j):
        a, b = ORDER[i], ORDER[j]
        return K[:, pair_index(a, b)] if a < b else K[:, pair_index(b, a)].T

    for s, (kind, n, m, q) in enumerate(STEPS):
        if kind == "full":
            for f in range(2):
                for r in range(2):
                    kstream[:, s, f, r] = weights(*TILES[q + f][r])
        else:
            for f in range(2):
                kstream[:, s, f, f] = weights(*TILES[q][f])
    kstream = kstream.reshape(EMBED, CHUNKS, CHUNK, STEP_COLS)
    W1 = a["W_top1"]
    w1 = np.zeros((P, GROUPS, HID1), W1.dtype)
    for q, pairs in enumerate(TILES):
        g, row = z_row(q)
        for r in range(2):
            w1[row + r, g] = W1[pair_index(*sorted(ORDER[i] for i in pairs[r]))]
    w1[DENSE_ROW:, GROUPS - 1] = W1[-DENSE:]
    consts = np.zeros((P, P + SEL + 32 + HOT_TILES), np.float32)
    consts[:, P + SEL + 32:] = np.arange(P * HOT_TILES).reshape(P, HOT_TILES)
    hot_tables = np.zeros((HOT_FIELDS, P * HOT_TILES, EMBED), K.dtype)
    for i, f in enumerate(SMALL):
        hot_tables[i, 0:TABLE_ROWS[f]] = a[f"tbl_{f}"]
    consts[:, 0:P] = np.eye(P, dtype=np.float32)
    for r in range(2):
        consts[64 * r:64 * r + 64, P + SEL + r] = 1.0

    def chunks(w, n):
        return np.ascontiguousarray(w.reshape(n, P, -1).transpose(1, 0, 2))

    arrays = {
        "dense_t": np.ascontiguousarray(a["dense_ctx"].T),
        "ids": a["ids"],
        "hot_ids": np.ascontiguousarray(a["ids"].T[SMALL]),
        "hot_tables": hot_tables.reshape(HOT_FIELDS, P, HOT_TILES, EMBED),
        "w1": w1,
        "b1": np.ascontiguousarray(a["b_top1"].reshape(-1, P).T),
        "w2": chunks(a["W_top2"], HID1 // P),
        "b2": np.ascontiguousarray(a["b_top2"].reshape(-1, P).T),
        "w3": np.ascontiguousarray(a["W_top3"].reshape(-1, P).T),
        "kstream": kstream,
        "consts": consts,
    }
    for f in ORDER[HOT_FIELDS:]:
        arrays[f"tbl_{f}"] = a[f"tbl_{f}"]
    nc = bacc.Bacc("TRN2", target_bir_lowering=False, num_devices=1)
    h = {k: nc.dram_tensor(k, v.shape, mybir.dt.from_np(v.dtype), kind="ExternalInput").ap()
         for k, v in arrays.items()}
    out = nc.dram_tensor("out", (BATCH, 1), mybir.dt.float32, kind="ExternalOutput").ap()
    build(nc, h["dense_t"], h["ids"], h["hot_ids"], h["hot_tables"],
          {f: h[f"tbl_{f}"] for f in ORDER[HOT_FIELDS:]}, h["w1"], h["b1"], h["w2"],
          h["b2"], h["w3"], h["kstream"], h["consts"], out.rearrange("b o -> o b"))
    got = run_bass_kernel_spmd(nc, [arrays], core_ids=[0])
    return got.results[0]["out"]
```
